# Optimizing a Trainium2 kernel written in Bass

```python
import numpy as np
import jax
import jax.numpy as jnp

def _softmax(x, axis=-1):
    return jax.nn.softmax(x, axis=axis)

def _gelu(x):
    return jax.nn.gelu(x, approximate=True)

def _silu(x):
    return jax.nn.silu(x)

def _sigmoid(x):
    return jax.nn.sigmoid(x)

def _layernorm(x, axis=-1, eps=1e-05):
    m = jnp.mean(x, axis=axis, keepdims=True)
    v = jnp.var(x, axis=axis, keepdims=True)
    return (x - m) / jnp.sqrt(v + eps)

def _scatter_add(tgt, idx, src, axis=0):
    return tgt.at[idx].add(src)

def _segment_sum(src, seg, n):
    return jax.ops.segment_sum(src, seg, n)
kernel_name = 'mk_dlrm_tower_d1_rec_r8_303dd6'

def setup_inputs(seed: int=0):
    np.random.seed(seed)
    _w = jnp.asarray

    def _rec_inputs():
        import jax
        import jax.numpy as jnp
        _tk = jax.random.key(seed)
        dense_ctx = jax.random.normal(jax.random.fold_in(_tk, 190), (1024, 16), jnp.float32)
        ids = jnp.stack([jax.random.randint(jax.random.fold_in(_tk, 200 + f), (1024,), 0, v, jnp.int32) for f, v in enumerate([12500, 125000, 1000, 12500, 12500, 125000, 12500, 125000, 1000, 1000, 1000, 1000, 1250, 1000, 1250, 12500, 1250, 1000, 12500, 1250, 12500, 12500, 1250, 1000, 1250, 1250, 1000, 1000, 1000, 1000, 1000, 1000])], axis=1)
        tbl_0 = 0.05 * jax.random.normal(jax.random.fold_in(_tk, 500 + 0), (12500, 64), jnp.float32)
        tbl_1 = 0.05 * jax.random.normal(jax.random.fold_in(_tk, 500 + 1), (125000, 64), jnp.float32)
        tbl_2 = 0.05 * jax.random.normal(jax.random.fold_in(_tk, 500 + 2), (1000, 64), jnp.float32)
        tbl_3 = 0.05 * jax.random.normal(jax.random.fold_in(_tk, 500 + 3), (12500, 64), jnp.float32)
        tbl_4 = 0.05 * jax.random.normal(jax.random.fold_in(_tk, 500 + 4), (12500, 64), jnp.float32)
        tbl_5 = 0.05 * jax.random.normal(jax.random.fold_in(_tk, 500 + 5), (125000, 64), jnp.float32)
        tbl_6 = 0.05 * jax.random.normal(jax.random.fold_in(_tk, 500 + 6), (12500, 64), jnp.float32)
        tbl_7 = 0.05 * jax.random.normal(jax.random.fold_in(_tk, 500 + 7), (125000, 64), jnp.float32)
        tbl_8 = 0.05 * jax.random.normal(jax.random.fold_in(_tk, 500 + 8), (1000, 64), jnp.float32)
        tbl_9 = 0.05 * jax.random.normal(jax.random.fold_in(_tk, 500 + 9), (1000, 64), jnp.float32)
        tbl_10 = 0.05 * jax.random.normal(jax.random.fold_in(_tk, 500 + 10), (1000, 64), jnp.float32)
        tbl_11 = 0.05 * jax.random.normal(jax.random.fold_in(_tk, 500 + 11), (1000, 64), jnp.float32)
        tbl_12 = 0.05 * jax.random.normal(jax.random.fold_in(_tk, 500 + 12), (1250, 64), jnp.float32)
        tbl_13 = 0.05 * jax.random.normal(jax.random.fold_in(_tk, 500 + 13), (1000, 64), jnp.float32)
        tbl_14 = 0.05 * jax.random.normal(jax.random.fold_in(_tk, 500 + 14), (1250, 64), jnp.float32)
        tbl_15 = 0.05 * jax.random.normal(jax.random.fold_in(_tk, 500 + 15), (12500, 64), jnp.float32)
        tbl_16 = 0.05 * jax.random.normal(jax.random.fold_in(_tk, 500 + 16), (1250, 64), jnp.float32)
        tbl_17 = 0.05 * jax.random.normal(jax.random.fold_in(_tk, 500 + 17), (1000, 64), jnp.float32)
        tbl_18 = 0.05 * jax.random.normal(jax.random.fold_in(_tk, 500 + 18), (12500, 64), jnp.float32)
        tbl_19 = 0.05 * jax.random.normal(jax.random.fold_in(_tk, 500 + 19), (1250, 64), jnp.float32)
        tbl_20 = 0.05 * jax.random.normal(jax.random.fold_in(_tk, 500 + 20), (12500, 64), jnp.float32)
        tbl_21 = 0.05 * jax.random.normal(jax.random.fold_in(_tk, 500 + 21), (12500, 64), jnp.float32)
        tbl_22 = 0.05 * jax.random.normal(jax.random.fold_in(_tk, 500 + 22), (1250, 64), jnp.float32)
        tbl_23 = 0.05 * jax.random.normal(jax.random.fold_in(_tk, 500 + 23), (1000, 64), jnp.float32)
        tbl_24 = 0.05 * jax.random.normal(jax.random.fold_in(_tk, 500 + 24), (1250, 64), jnp.float32)
        tbl_25 = 0.05 * jax.random.normal(jax.random.fold_in(_tk, 500 + 25), (1250, 64), jnp.float32)
        tbl_26 = 0.05 * jax.random.normal(jax.random.fold_in(_tk, 500 + 26), (1000, 64), jnp.float32)
        tbl_27 = 0.05 * jax.random.normal(jax.random.fold_in(_tk, 500 + 27), (1000, 64), jnp.float32)
        tbl_28 = 0.05 * jax.random.normal(jax.random.fold_in(_tk, 500 + 28), (1000, 64), jnp.float32)
        tbl_29 = 0.05 * jax.random.normal(jax.random.fold_in(_tk, 500 + 29), (1000, 64), jnp.float32)
        tbl_30 = 0.05 * jax.random.normal(jax.random.fold_in(_tk, 500 + 30), (1000, 64), jnp.float32)
        tbl_31 = 0.05 * jax.random.normal(jax.random.fold_in(_tk, 500 + 31), (1000, 64), jnp.float32)
        _rk = jax.random.fold_in(_tk, 7)
        W_top1 = 0.0441942 * jax.random.normal(jax.random.fold_in(_tk, 801), (512, 512), jnp.float32)
        W_top2 = 0.0441942 * jax.random.normal(jax.random.fold_in(_tk, 802), (512, 256), jnp.float32)
        W_top3 = 0.0625 * jax.random.normal(jax.random.fold_in(_tk, 803), (256, 1), jnp.float32)
        b_top1 = jnp.zeros((512,), jnp.float32)
        b_top2 = jnp.zeros((256,), jnp.float32)
        return (dense_ctx, ids, tbl_0, tbl_1, tbl_2, tbl_3, tbl_4, tbl_5, tbl_6, tbl_7, tbl_8, tbl_9, tbl_10, tbl_11, tbl_12, tbl_13, tbl_14, tbl_15, tbl_16, tbl_17, tbl_18, tbl_19, tbl_20, tbl_21, tbl_22, tbl_23, tbl_24, tbl_25, tbl_26, tbl_27, tbl_28, tbl_29, tbl_30, tbl_31, W_top1, b_top1, W_top2, b_top2, W_top3)
    dense_ctx, ids, tbl_0, tbl_1, tbl_2, tbl_3, tbl_4, tbl_5, tbl_6, tbl_7, tbl_8, tbl_9, tbl_10, tbl_11, tbl_12, tbl_13, tbl_14, tbl_15, tbl_16, tbl_17, tbl_18, tbl_19, tbl_20, tbl_21, tbl_22, tbl_23, tbl_24, tbl_25, tbl_26, tbl_27, tbl_28, tbl_29, tbl_30, tbl_31, W_top1, b_top1, W_top2, b_top2, W_top3 = _rec_inputs()

    def _L0_rec_setup():
        import jax, jax.numpy as jnp
        import numpy as np
        B = 256
        NUM_FIELDS = 32
        EMBED = 64
        P = NUM_FIELDS * (NUM_FIELDS - 1) // 2
        _ROW, _COL = np.triu_indices(NUM_FIELDS, k=1)
        ROW_IDX = jnp.asarray(_ROW, dtype=jnp.int32)
        COL_IDX = jnp.asarray(_COL, dtype=jnp.int32)
        key = jax.random.key(seed)
        k1, k2 = jax.random.split(key)
        emb_inputs = jax.random.normal(k1, (B, NUM_FIELDS, EMBED), dtype=jnp.float32)
        fan_in = P * EMBED
        fan_out = EMBED
        std = float(np.sqrt(2.0 / (fan_in + fan_out)))
        kernel = jax.random.normal(k2, (EMBED, P, EMBED), dtype=jnp.float32) * std
        return {'emb_inputs': emb_inputs, 'kernel': kernel}
    _L0_rec_all = _L0_rec_setup()
    _L0_rec_in = {k: v for k, v in _L0_rec_all.items() if k in ('kernel',)}
    del _L0_rec_all
    return {'dense_ctx': dense_ctx, 'ids': ids, 'tbl_0': tbl_0, 'tbl_1': tbl_1, 'tbl_2': tbl_2, 'tbl_3': tbl_3, 'tbl_4': tbl_4, 'tbl_5': tbl_5, 'tbl_6': tbl_6, 'tbl_7': tbl_7, 'tbl_8': tbl_8, 'tbl_9': tbl_9, 'tbl_10': tbl_10, 'tbl_11': tbl_11, 'tbl_12': tbl_12, 'tbl_13': tbl_13, 'tbl_14': tbl_14, 'tbl_15': tbl_15, 'tbl_16': tbl_16, 'tbl_17': tbl_17, 'tbl_18': tbl_18, 'tbl_19': tbl_19, 'tbl_20': tbl_20, 'tbl_21': tbl_21, 'tbl_22': tbl_22, 'tbl_23': tbl_23, 'tbl_24': tbl_24, 'tbl_25': tbl_25, 'tbl_26': tbl_26, 'tbl_27': tbl_27, 'tbl_28': tbl_28, 'tbl_29': tbl_29, 'tbl_30': tbl_30, 'tbl_31': tbl_31, 'W_top1': W_top1, 'b_top1': b_top1, 'W_top2': W_top2, 'b_top2': b_top2, 'W_top3': W_top3, 'L0_rec_kernel': _L0_rec_in['kernel']}

def reference(dense_ctx, ids, tbl_0, tbl_1, tbl_2, tbl_3, tbl_4, tbl_5, tbl_6, tbl_7, tbl_8, tbl_9, tbl_10, tbl_11, tbl_12, tbl_13, tbl_14, tbl_15, tbl_16, tbl_17, tbl_18, tbl_19, tbl_20, tbl_21, tbl_22, tbl_23, tbl_24, tbl_25, tbl_26, tbl_27, tbl_28, tbl_29, tbl_30, tbl_31, W_top1, b_top1, W_top2, b_top2, W_top3, L0_rec_kernel):
    import jax
    import jax.numpy as jnp

    def _L0_rec_ref(emb_inputs, kernel):
        import jax, jax.numpy as jnp
        import numpy as np
        B = 256
        NUM_FIELDS = 32
        EMBED = 64
        P = NUM_FIELDS * (NUM_FIELDS - 1) // 2
        _ROW, _COL = np.triu_indices(NUM_FIELDS, k=1)
        ROW_IDX = jnp.asarray(_ROW, dtype=jnp.int32)
        COL_IDX = jnp.asarray(_COL, dtype=jnp.int32)
        p = emb_inputs[:, ROW_IDX]
        q = emb_inputs[:, COL_IDX]
        return jnp.einsum('bne,hne,bnh->bn', p, kernel, q)
    e = jnp.stack([tbl_0[ids[:, 0]], tbl_1[ids[:, 1]], tbl_2[ids[:, 2]], tbl_3[ids[:, 3]], tbl_4[ids[:, 4]], tbl_5[ids[:, 5]], tbl_6[ids[:, 6]], tbl_7[ids[:, 7]], tbl_8[ids[:, 8]], tbl_9[ids[:, 9]], tbl_10[ids[:, 10]], tbl_11[ids[:, 11]], tbl_12[ids[:, 12]], tbl_13[ids[:, 13]], tbl_14[ids[:, 14]], tbl_15[ids[:, 15]], tbl_16[ids[:, 16]], tbl_17[ids[:, 17]], tbl_18[ids[:, 18]], tbl_19[ids[:, 19]], tbl_20[ids[:, 20]], tbl_21[ids[:, 21]], tbl_22[ids[:, 22]], tbl_23[ids[:, 23]], tbl_24[ids[:, 24]], tbl_25[ids[:, 25]], tbl_26[ids[:, 26]], tbl_27[ids[:, 27]], tbl_28[ids[:, 28]], tbl_29[ids[:, 29]], tbl_30[ids[:, 30]], tbl_31[ids[:, 31]]], axis=1)
    z = _L0_rec_ref(e, L0_rec_kernel)
    z = z.reshape(z.shape[0], -1)
    h = jnp.concatenate([z, dense_ctx], axis=1)
    h = jnp.maximum(h @ W_top1 + b_top1, 0.0)
    h = jnp.maximum(h @ W_top2 + b_top2, 0.0)
    y = h @ W_top3
    return y

_drawn_inputs = setup_inputs


def setup_inputs(seed=0):
    import zlib

    import numpy as np

    out = dict(_drawn_inputs(seed))
    spreads = {'b_top1': (0.0, 0.1), 'b_top2': (0.0, 0.1)}
    factors = {'tbl_0': 8.0,
     'tbl_1': 8.0,
     'tbl_2': 8.0,
     'tbl_3': 8.0,
     'tbl_4': 8.0,
     'tbl_5': 8.0,
     'tbl_6': 8.0,
     'tbl_7': 8.0,
     'tbl_8': 8.0,
     'tbl_9': 8.0,
     'tbl_10': 8.0,
     'tbl_11': 8.0,
     'tbl_12': 8.0,
     'tbl_13': 8.0,
     'tbl_14': 8.0,
     'tbl_15': 8.0,
     'tbl_16': 8.0,
     'tbl_17': 8.0,
     'tbl_18': 8.0,
     'tbl_19': 8.0,
     'tbl_20': 8.0,
     'tbl_21': 8.0,
     'tbl_22': 8.0,
     'tbl_23': 8.0,
     'tbl_24': 8.0,
     'tbl_25': 8.0,
     'tbl_26': 8.0,
     'tbl_27': 8.0,
     'tbl_28': 8.0,
     'tbl_29': 8.0,
     'tbl_30': 8.0,
     'tbl_31': 8.0,
     'L0_rec_kernel': 8.0}
    for name, (base, spread) in spreads.items():
        noise = np.random.default_rng([zlib.crc32(name.encode()), seed]).standard_normal(out[name].shape)
        drawn = base * np.exp(spread * noise) if base else spread * noise
        out[name] = jnp.asarray(drawn.astype(out[name].dtype))
    for name, factor in factors.items():
        out[name] = (out[name] * factor).astype(out[name].dtype)
    return out
```

```python
from contextlib import ExitStack

import numpy as np

import concourse.bass as bass
from concourse import mybir

F32 = mybir.dt.float32
F32R = mybir.dt.float32r
I32 = mybir.dt.int32
ALU = mybir.AluOpType
ACT = mybir.ActivationFunctionType
AX_X = mybir.AxisListType.X

P = 128
FIELDS = 32
EMBED = 64
BATCH = 1024
DENSE = 16
HID1, HID2 = 512, 256
TILES = BATCH // P
PAIRS = FIELDS * (FIELDS - 1) // 2
BANK = 8
FULL = 2 * BANK
GROUP = 4
GROUPS = FIELDS // GROUP
AHEAD = 3
DSLOTS = AHEAD + 1
CHUNK = BANK
CHUNKS = PAIRS // CHUNK
KSLOTS = 4
USLOTS = 3
K_AHEAD = 3


def pair(j, i):
    return j * (j - 1) // 2 + i


def plan_blocks():
    groups = []
    for g in range(GROUPS):
        blocks = []
        for j in range(GROUP * g, GROUP * g + GROUP):
            if j == 0:
                continue
            if j > FULL:
                n = BANK if j - BANK <= FULL else FULL
                blocks += [[(j, 0, n)], [(j, n, j - n)]]
            elif blocks and sum(n for _, _, n in blocks[-1]) + j <= FULL:
                blocks[-1].append((j, 0, j))
            else:
                blocks.append([(j, 0, j)])
        groups.append(blocks)
    return groups


GROUP_BLOCKS = plan_blocks()
BLOCKS = [b for g in GROUP_BLOCKS for b in g]
NB = len(BLOCKS)
FIRST = [sum(len(b) for b in GROUP_BLOCKS[:g]) for g in range(GROUPS + 1)]
WIDTH = [sum(n for _, _, n in b) for b in BLOCKS]
START = [sum(WIDTH[:k]) for k in range(NB + 1)]
PSLOTS = 4
ACT_SHARE = 0.40
ON_ACT = [round(w * ACT_SHARE) for w in WIDTH]
assert NB % USLOTS == 0 and 2 * NB % PSLOTS == 0


def product_slot(u, k):
    return (u * NB + k) % PSLOTS


MLP_AT = {3: 0, 4: 1, 5: 2, 6: 3}


def chunks_for(k):
    return -(-START[min(k, NB - 1) + 1] // CHUNK)


def turn_block(g):
    return min(FIRST[g] + USLOTS, FIRST[g + 1]) - 1


def build(nc, ids, tables, k_pairs, dense, w1, b1, w2, b2, w3, ident, out):
    with ExitStack() as ctx:
        def sb(name, shape, dt=F32):
            return ctx.enter_context(nc.sbuf_tensor(name, shape, dt))

        def sem(name):
            return ctx.enter_context(nc.semaphore(name))

        k_split = sb("k_split", [P, PAIRS * EMBED], F32R)
        k_raw = sb("k_raw", [EMBED, KSLOTS, CHUNK * EMBED])
        emb = [sb(f"emb{u}", [P, FIELDS * EMBED]) for u in range(2)]
        split_t = sb("split_t", [P, 2, GROUP // 2, 2, P], F32R)
        twice_t = sb("twice_t", [P, DSLOTS, GROUP // 2, 2, 2, P], F32R)
        prod = sb("prod", [P, PSLOTS, FULL * EMBED])
        h0 = [sb(f"h0_{u}", [P, 512]) for u in range(2)]
        h0_t = sb("h0_t", [P, 4, P])
        h1_t = sb("h1_t", [P, 4, P])
        h2_t = sb("h2_t", [P, 2, P])
        y_row = sb("y_row", [1, P])
        w1_sb = sb("w1_sb", [P, 4, HID1])
        w2_sb = sb("w2_sb", [P, 4, HID2])
        w3_sb = sb("w3_sb", [P, 2])
        b1_sb = sb("b1_sb", [P, 4])
        b2_sb = sb("b2_sb", [P, 2])
        id_sb = sb("id_sb", [P, P])
        ids_all = sb("ids_all", [P, TILES, FIELDS], I32)
        ids_now = [sb(f"ids_now{u}", [P, FIELDS], I32) for u in range(2)]

        u_ps = [ctx.enter_context(nc.psum_tensor(f"u_ps{s}", [P, FULL * EMBED], F32)) for s in range(USLOTS)]
        t_ps = ctx.enter_context(nc.psum_tensor("t_ps", [P, 512], F32))[:, 0:GROUP // 2 * P].rearrange(
            "p (m b) -> p m b", b=P)
        mlp_ps = ctx.enter_context(nc.psum_tensor("mlp_ps", [P, 4, P], F32))

        ids_loaded = sem("ids_loaded")
        ids_copied = sem("ids_copied")
        id_loaded = sem("id_loaded")
        weights_loaded = sem("weights_loaded")
        dense_loaded = [sem(f"dense_loaded{u}") for u in range(2)]
        gathered = [[sem(f"gathered{u}_{g}") for g in range(GROUPS)] for u in range(2)]
        k_loaded = [sem(f"k_loaded{s}") for s in range(KSLOTS)]
        k_hi_done = sem("k_hi_done")
        k_lo_done = sem("k_lo_done")
        transposed = sem("transposed")
        hi_done = sem("hi_done")
        lo_done = sem("lo_done")
        doubled = [sem(f"doubled{s}") for s in range(DSLOTS)]
        u_ready = sem("u_ready")
        multiplied = sem("multiplied")
        summed_v = sem("summed_v")
        summed_a = sem("summed_a")
        mlp_mm = sem("mlp_mm")
        mlp_out = sem("mlp_out")
        stored = sem("stored")

        block = ctx.enter_context(nc.Block())

        @block.gpsimd
        def _(pool):
            pool.wait_ge(ids_loaded, 16)

            copies_register = pool.alloc_register("copies")

            def tile(t, u):
                copies = t + 1
                if not isinstance(t, int):
                    pool.reg_mov(copies_register, t + 1)
                    copies = pool.snap(copies_register)
                nc.gpsimd.tensor_copy(ids_now[u][:], ids_all[:, t, :]).then_inc(ids_copied, 1)
                pool.wait_ge(ids_loaded, 16)
                pool.wait_ge(ids_copied, copies)
                for f in range(FIELDS):
                    nc.gpsimd.indirect_dma_start(
                        emb[u][:, f * EMBED:(f + 1) * EMBED], None, tables[f],
                        bass.IndirectOffsetOnAxis(ap=ids_now[u][:, f:f + 1], axis=0),
                    ).then_inc(gathered[u][f // GROUP], 16)

            tile(0, 0)
            tile(1, 1)
            with pool.Fori(1, TILES // 2) as it:
                for u in range(2):
                    t = 2 * it + u
                    pool.wait_ge(multiplied, (t - 1) * NB)
                    tile(t, u)

        @block.sync
        def _(sp):
            sp.dma_start(ids_all[:], ids.rearrange("(t p) f -> p t f", p=P)).then_inc(ids_loaded, 16)
            sp.dma_start(id_sb[:], ident).then_inc(id_loaded, 16)

            def double(t, g):
                sp.wait_ge(lo_done, t * GROUPS + g + 1)
                for parity in range(2):
                    for half in range(2):
                        sp.dma_start(
                            twice_t[half * EMBED:(half + 1) * EMBED, g % DSLOTS, :, parity].bitcast(F32),
                            split_t[parity * EMBED:(parity + 1) * EMBED, g % 2].bitcast(F32),
                        ).then_inc(doubled[g % DSLOTS], 16)

            def load_dense(t, u):
                sp.dma_start(h0[u][:, PAIRS:], dense[bass.ts(t, P), :]).then_inc(dense_loaded[u], 16)

            def tile(t, u, last=False):
                for g in range(GROUPS):
                    if g + AHEAD < GROUPS:
                        double(t, g + AHEAD)
                    elif not last:
                        double(t + 1, g + AHEAD - GROUPS)
                    if g == 1:
                        load_dense(t, u)

            for g in range(AHEAD):
                double(0, g)
            sp.dma_start(w1_sb[:], w1.rearrange("(c p) n -> p c n", p=P)).then_inc(weights_loaded, 16)
            sp.dma_start(w2_sb[:], w2.rearrange("(c p) n -> p c n", p=P)).then_inc(weights_loaded, 16)
            sp.dma_start(w3_sb[:], w3).then_inc(weights_loaded, 16)
            sp.dma_start(b1_sb[:], b1).then_inc(weights_loaded, 16)
            sp.dma_start(b2_sb[:], b2).then_inc(weights_loaded, 16)
            tile(0, 0)
            with sp.Fori(1, TILES - 1, 2) as t1:
                for d in range(2):
                    tile(t1 + d, (1 + d) % 2)
            tile(TILES - 1, (TILES - 1) % 2, last=True)
            sp.wait_ge(stored, 16 * TILES)

        @block.scalar
        def _(act):
            act.sem_inc(mlp_out, 1)

            def load_k(c):
                act.dma_start(
                    k_raw[:, c % KSLOTS], k_pairs[:, c * CHUNK * EMBED:(c + 1) * CHUNK * EMBED],
                ).then_inc(k_loaded[c % KSLOTS], 16)

            k_next = [0]

            def round_k(upto):
                while k_next[0] < min(upto, CHUNKS):
                    c = k_next[0]
                    act.wait_ge(k_loaded[c % KSLOTS], 16 * (c // KSLOTS + 1))
                    nc.scalar.activation(
                        k_split[0:EMBED, c * CHUNK * EMBED:(c + 1) * CHUNK * EMBED], k_raw[:, c % KSLOTS], ACT.Copy,
                    ).then_inc(k_hi_done, 1)
                    if c >= 2 and c - 2 + KSLOTS < CHUNKS:
                        act.wait_ge(k_lo_done, c - 1)
                        load_k(c - 2 + KSLOTS)
                    k_next[0] += 1

            def round_group(t, g, reused=True):
                act.wait_ge(transposed, t * GROUPS + g + 1)
                if reused:
                    before = g - 2 if g >= 2 else g - 2 + GROUPS
                    turn = (t if g >= 2 else t - 1) * (GROUPS // DSLOTS) + before // DSLOTS
                    act.wait_ge(doubled[before % DSLOTS], 64 * (turn + 1))
                nc.scalar.activation(split_t[:, g % 2, :, 0], t_ps, ACT.Copy).then_inc(hi_done, 1)

            def sum_block(t, u, k):
                act.wait_ge(multiplied, t * NB + k + 1)
                for n in range(ON_ACT[k]):
                    product = prod[:, product_slot(u, k), n * EMBED:(n + 1) * EMBED]
                    last = nc.scalar.activation(product, product, ACT.Copy,
                                                accum_out=h0[u][:, START[k] + n:START[k] + n + 1])
                last.then_inc(summed_a, 1)

            def mlp_step(t, step):
                act.wait_ge(mlp_mm, 4 * t + step + 1)
                if step == 0:
                    last = nc.scalar.activation(h0_t[:], mlp_ps[:], ACT.Copy)
                elif step == 1:
                    for m in range(4):
                        last = nc.scalar.activation(h1_t[:, m], mlp_ps[:, m], ACT.Relu, bias=b1_sb[:, m:m + 1])
                elif step == 2:
                    for m in range(2):
                        last = nc.scalar.activation(h2_t[:, m], mlp_ps[:, m], ACT.Relu, bias=b2_sb[:, m:m + 1])
                else:
                    act.wait_ge(stored, 16 * t)
                    last = nc.scalar.activation(y_row[:], mlp_ps[0:1, 0], ACT.Copy)
                last.then_inc(mlp_out, 1)
                if step == 3:
                    act.wait_ge(mlp_out, 4 * t + 5)
                    act.dma_start(out[:, bass.ts(t, P)], y_row[:]).then_inc(stored, 16)

            def tile(t, u, first=False, last=False):
                for g in range(GROUPS):
                    if first:
                        round_k(chunks_for(FIRST[g] + K_AHEAD))
                    if not first and g in MLP_AT:
                        mlp_step(t - 1, MLP_AT[g])
                    for k in range(FIRST[g], FIRST[g + 1]):
                        if first:
                            round_k(chunks_for(k + K_AHEAD + 1))
                        if k == min(turn_block(g) + 1, FIRST[g + 1] - 1):
                            if g + AHEAD < GROUPS:
                                round_group(t, g + AHEAD)
                            elif not last:
                                round_group(t + 1, g + AHEAD - GROUPS)
                        sum_block(t, u, k)

            for c in range(KSLOTS):
                load_k(c)
            round_k(chunks_for(0))
            for g in range(AHEAD):
                round_group(0, g, reused=g >= 2)
            act.wait_ge(weights_loaded, 80)
            tile(0, 0, first=True)
            with act.Fori(1, TILES - 1, 2) as t1:
                for d in range(2):
                    tile(t1 + d, (1 + d) % 2)
            tile(TILES - 1, (TILES - 1) % 2, last=True)
            for step in range(4):
                mlp_step(TILES - 1, step)

        @block.vector
        def _(dve):
            k_next = [0]

            def split_k(upto):
                while k_next[0] < min(upto, CHUNKS):
                    c = k_next[0]
                    cols = slice(c * CHUNK * EMBED, (c + 1) * CHUNK * EMBED)
                    dve.wait_ge(k_hi_done, c + 1)
                    nc.vector.tensor_tensor(k_split[EMBED:P, cols], k_raw[:, c % KSLOTS],
                                            k_split[0:EMBED, cols].bitcast(F32), ALU.subtract).then_inc(k_lo_done, 1)
                    k_next[0] += 1

            def split_group(t, g):
                dve.wait_ge(hi_done, t * GROUPS + g + 1)
                nc.vector.tensor_tensor(split_t[:, g % 2, :, 1], t_ps,
                                        split_t[:, g % 2, :, 0].bitcast(F32), ALU.subtract).then_inc(lo_done, 1)

            def multiply(t, u, k):
                dve.wait_ge(u_ready, t * NB + k + 1)
                if k >= PSLOTS or not isinstance(t, int) or t > 0:
                    dve.wait_ge(summed_a, t * NB + k + 1 - PSLOTS)
                    dve.wait_ge(summed_v, t * NB + k + 1 - PSLOTS)
                product = prod[:, product_slot(u, k)]
                at = 0
                for j, i, n in BLOCKS[k]:
                    cols = slice(at * EMBED, (at + n) * EMBED)
                    last = nc.vector.tensor_tensor(product[:, cols], u_ps[k % USLOTS][:, cols],
                                                   emb[u][:, i * EMBED:(i + n) * EMBED], ALU.mult)
                    at += n
                last.then_inc(multiplied, 1)

            def sum_block(t, u, k):
                dve.wait_ge(multiplied, t * NB + k + 1)
                product = prod[:, product_slot(u, k), ON_ACT[k] * EMBED:WIDTH[k] * EMBED]
                nc.vector.tensor_reduce(h0[u][:, START[k] + ON_ACT[k]:START[k + 1]],
                                        product.rearrange("p (n e) -> p n e", e=EMBED), AX_X, ALU.add,
                                        ).then_inc(summed_v, 1)

            def tile(t, u, first=False, last=False):
                for g in range(GROUPS):
                    for k in range(FIRST[g], FIRST[g + 1]):
                        if first:
                            split_k(chunks_for(k + K_AHEAD))
                        if k == FIRST[g + 1] - 1:
                            if g + AHEAD < GROUPS:
                                split_group(t, g + AHEAD)
                            elif not last:
                                split_group(t + 1, g + AHEAD - GROUPS)
                        multiply(t, u, k)
                        if k > 0:
                            sum_block(t, u, k - 1)
                sum_block(t, u, NB - 1)

            split_k(chunks_for(0))
            for g in range(AHEAD):
                split_group(0, g)
            tile(0, 0, first=True)
            with dve.Fori(1, TILES - 1, 2) as t1:
                for d in range(2):
                    tile(t1 + d, (1 + d) % 2)
            tile(TILES - 1, (TILES - 1) % 2, last=True)

        @block.tensor
        def _(pe):
            def transpose_group(t, g, u):
                turn = (t // 2 if isinstance(t, int) else (t - u) // 2) + 1
                pe.wait_ge(gathered[u][g], 16 * GROUP * turn)
                if g > 0 or not isinstance(t, int) or t > 0:
                    pe.wait_ge(lo_done, t * GROUPS + g)
                for m in range(GROUP // 2):
                    f = GROUP * g + 2 * m
                    last = nc.tensor.transpose(t_ps[:, m], emb[u][:, f * EMBED:(f + 2) * EMBED], id_sb[:])
                last.then_inc(transposed, 1)

            def block_u(t, k):
                if k >= USLOTS or not isinstance(t, int) or t > 0:
                    pe.wait_ge(multiplied, t * NB + k + 1 - USLOTS)
                at = 0
                for j, i, n in BLOCKS[k]:
                    slot = j // GROUP % DSLOTS
                    done = 0
                    while done < n:
                        m = min(n - done, BANK - (at + done) % BANK)
                        dst = u_ps[k % USLOTS][:, (at + done) * EMBED:(at + done + m) * EMBED]
                        src = k_split[:, (pair(j, i) + done) * EMBED:(pair(j, i) + done + m) * EMBED]
                        for part in range(2):
                            last = nc.tensor.matmul(dst, twice_t[:, slot, j % GROUP // 2, j % 2, part], src,
                                                    start=(part == 0), stop=(part == 1))
                        done += m
                    at += n
                last.then_inc(u_ready, 1)

            def mlp_step(t, u, step):
                pe.wait_ge(mlp_out, 4 * t + step + 1)
                if step == 0:
                    pe.wait_ge(summed_v, (t + 1) * NB)
                    pe.wait_ge(summed_a, (t + 1) * NB)
                    turn = (t // 2 if isinstance(t, int) else (t - u) // 2) + 1
                    pe.wait_ge(dense_loaded[u], 16 * turn)
                    for c in range(4):
                        last = nc.tensor.transpose(mlp_ps[:, c], h0[u][:, c * P:(c + 1) * P], id_sb[:])
                elif step == 1:
                    for m in range(4):
                        for c in range(4):
                            last = nc.tensor.matmul(mlp_ps[:, m], w1_sb[:, c, m * P:(m + 1) * P], h0_t[:, c],
                                                    start=(c == 0), stop=(c == 3))
                elif step == 2:
                    for m in range(2):
                        for c in range(4):
                            last = nc.tensor.matmul(mlp_ps[:, m], w2_sb[:, c, m * P:(m + 1) * P], h1_t[:, c],
                                                    start=(c == 0), stop=(c == 3))
                else:
                    for c in range(2):
                        last = nc.tensor.matmul(mlp_ps[0:1, 0], w3_sb[:, c:c + 1], h2_t[:, c],
                                                start=(c == 0), stop=(c == 1))
                last.then_inc(mlp_mm, 1)

            def tile(t, u, first=False, last=False):
                for g in range(GROUPS):
                    if not first and g in MLP_AT:
                        mlp_step(t - 1, 1 - u, MLP_AT[g])
                    pe.wait_ge(doubled[g % DSLOTS], 64 * (t * (GROUPS // DSLOTS) + g // DSLOTS + 1))
                    for k in range(FIRST[g], FIRST[g + 1]):
                        if first:
                            pe.wait_ge(k_lo_done, chunks_for(k))
                        block_u(t, k)
                        if k == turn_block(g):
                            if g + AHEAD < GROUPS:
                                transpose_group(t, g + AHEAD, u)
                            elif not last:
                                transpose_group(t + 1, g + AHEAD - GROUPS, 1 - u)

            pe.wait_ge(id_loaded, 16)
            for g in range(AHEAD):
                transpose_group(0, g, 0)
            pe.wait_ge(weights_loaded, 80)
            tile(0, 0, first=True)
            with pe.Fori(1, TILES - 1, 2) as t1:
                for d in range(2):
                    tile(t1 + d, (1 + d) % 2)
            tile(TILES - 1, (TILES - 1) % 2, last=True)
            for step in range(4):
                mlp_step(TILES - 1, (TILES - 1) % 2, step)


def by_partition(v):
    return np.ascontiguousarray(np.asarray(v).reshape(-1, P).T)


def kernel(**inputs):
    import concourse.bacc as bacc
    from concourse.bass_utils import run_bass_kernel_spmd

    order = [i * (2 * FIELDS - i - 1) // 2 + j - i - 1 for j in range(FIELDS) for i in range(j)]
    w1 = np.asarray(inputs["W_top1"])
    k = np.asarray(inputs["L0_rec_kernel"])
    arrays = {
        "ids": np.asarray(inputs["ids"]),
        "k_pairs": np.ascontiguousarray(k[:, order, :]).reshape(EMBED, PAIRS * EMBED),
        "dense": np.asarray(inputs["dense_ctx"]),
        "w1": np.concatenate([w1[:PAIRS][order], w1[PAIRS:]], axis=0),
        "b1": by_partition(inputs["b_top1"]),
        "w2": np.asarray(inputs["W_top2"]),
        "b2": by_partition(inputs["b_top2"]),
        "w3": by_partition(inputs["W_top3"]),
        "ident": np.eye(P, dtype=np.float32),
    }
    for f in range(FIELDS):
        arrays[f"tbl_{f}"] = np.asarray(inputs[f"tbl_{f}"])
    nc = bacc.Bacc("TRN2", target_bir_lowering=False, num_devices=1)
    ap = {n: nc.dram_tensor(n, a.shape, mybir.dt.from_np(a.dtype), kind="ExternalInput").ap()
          for n, a in arrays.items()}
    out = nc.dram_tensor("out", (1, BATCH), F32, kind="ExternalOutput").ap()
    build(nc, ap["ids"], [ap[f"tbl_{f}"] for f in range(FIELDS)], ap["k_pairs"], ap["dense"],
          ap["w1"], ap["b1"], ap["w2"], ap["b2"], ap["w3"], ap["ident"], out)
    r = run_bass_kernel_spmd(nc, [arrays], core_ids=[0])
    return r.results[0]["out"].reshape(BATCH, 1)
```

```python
from contextlib import ExitStack

import numpy as np

import concourse.bass as bass
from concourse import mybir

F32 = mybir.dt.float32
F32R = mybir.dt.float32r
I32 = mybir.dt.int32
ALU = mybir.AluOpType
ACT = mybir.ActivationFunctionType
AX_X = mybir.AxisListType.X

P = 128
FIELDS = 32
EMBED = 64
BATCH = 1024
DENSE = 16
HID1, HID2 = 512, 256
TILES = BATCH // P
PAIRS = FIELDS * (FIELDS - 1) // 2
BANK = 8
FULL = 2 * BANK
GROUP = 4
GROUPS = FIELDS // GROUP
AHEAD = 3
DSLOTS = AHEAD + 1
CHUNK = FULL
CHUNKS = PAIRS // CHUNK
USLOTS = 3
PSLOTS = 4
KSLOTS = PSLOTS * FULL // CHUNK
TURNED_FIELDS = [18, 20, 22, 24, 26, 28, 30, 31]
LOW = FULL // 2


def pair(j, i):
    return j * (j - 1) // 2 + i


def plan_blocks():
    groups = []
    for g in range(GROUPS):
        blocks = []
        for j in range(GROUP * g, GROUP * g + GROUP):
            if j == 0:
                continue
            if j > FULL:
                n = BANK if j - BANK <= FULL and j not in TURNED_FIELDS else FULL
                blocks += [[(j, 0, n)], [(j, n, j - n)]]
            elif blocks and sum(n for _, _, n in blocks[-1]) + j <= FULL:
                blocks[-1].append((j, 0, j))
            else:
                blocks.append([(j, 0, j)])
        groups.append(blocks)
    return groups


GROUP_BLOCKS = plan_blocks()
BLOCKS = [b for g in GROUP_BLOCKS for b in g]
NB = len(BLOCKS)
FIRST = [sum(len(b) for b in GROUP_BLOCKS[:g]) for g in range(GROUPS + 1)]
WIDTH = [sum(n for _, _, n in b) for b in BLOCKS]
START = [sum(WIDTH[:k]) for k in range(NB + 1)]
TURNED = [b[0][0] in TURNED_FIELDS and b[0][1] == 0 for b in BLOCKS]
NT = sum(TURNED)
NS = NB - NT
T_INDEX = [sum(TURNED[:k]) for k in range(NB)]
S_INDEX = [k - T_INDEX[k] for k in range(NB)]
COLUMN = [sum(w for w, t in zip(WIDTH[:k], TURNED) if not t) for k in range(NB)]
STRAIGHT = PAIRS - NT * FULL
SHARES = [0.5] * 4 + [0.55] * 4
ON_ACT = [min(WIDTH[k] - 1, round(WIDTH[k] * SHARES[BLOCKS[k][-1][0] // GROUP])) for k in range(NB)]
QUADS = 4
SUMS = FULL // 2 * NT
assert NB % USLOTS == 0 and 2 * NB % PSLOTS == 0
assert SUMS == QUADS * 16 and STRAIGHT + DENSE == 3 * P


def product_slot(u, k):
    return (u * NB + k) % PSLOTS


def w1_rows():
    straight = [(i, j) for k in range(NB) if not TURNED[k] for j, i0, n in BLOCKS[k] for i in range(i0, i0 + n)]
    turned = [None] * P
    for k in range(NB):
        if TURNED[k]:
            for i in range(FULL):
                g = T_INDEX[k] * LOW + i // 2
                turned[32 * (g % QUADS) + 2 * (g // QUADS) + i % 2] = (i, BLOCKS[k][0][0])
    rows = [i * (2 * FIELDS - i - 1) // 2 + j - i - 1 for i, j in straight]
    rows += range(PAIRS, PAIRS + DENSE)
    return rows + [i * (2 * FIELDS - i - 1) // 2 + j - i - 1 for i, j in turned]


MLP_AT = {4: 0, 6: 1, 9: 2, 12: 3, 15: 4}
STEPS = 5
TURN_AT = [0, 5, 10, 15, 20, 26, 31, 36]
ROUND_AT = {k + 1: g for g, k in enumerate(TURN_AT)}
SPLIT_AT = {k + USLOTS: g for g, k in enumerate(TURN_AT)}
assert all(TURN_AT[g + 1] >= TURN_AT[g] + USLOTS + 2 for g in range(GROUPS - 1))
assert all(FIRST[g] <= TURN_AT[g] + USLOTS < NB for g in range(GROUPS))
EARLY_AT = {9: 0, 14: 1, 19: 2}


def build(nc, ids, tables, k_pairs, dense, w1, b1, w2, b2, w3, ident, pick, out):
    with ExitStack() as ctx:
        def sb(name, shape, dt=F32):
            return ctx.enter_context(nc.sbuf_tensor(name, shape, dt))

        def sem(name):
            return ctx.enter_context(nc.semaphore(name))

        k_split = sb("k_split", [P, PAIRS * EMBED], F32R)
        emb = [sb(f"emb{u}", [P, FIELDS * EMBED]) for u in range(2)]
        split_t = sb("split_t", [P, 2, GROUP // 2, 2, P], F32R)
        twice_t = sb("twice_t", [P, DSLOTS, GROUP // 2, 2, 2, P], F32R)
        low_t = [sb(f"low_t{u}", [P, LOW, P]) for u in range(2)]
        prod = sb("prod", [P, PSLOTS, FULL * EMBED])
        k_raw = prod[0:EMBED].rearrange("p s (c n) -> p (s c) n", n=CHUNK * EMBED)
        h0 = [sb(f"h0_{u}", [P, STRAIGHT + DENSE]) for u in range(2)]
        h0_t = sb("h0_t", [P, 4, P])
        h1_t = sb("h1_t", [P, 4, P])
        h2_t = sb("h2_t", [P, 2, P])
        y_row = sb("y_row", [1, P])
        w1_sb = sb("w1_sb", [P, 4, HID1])
        w2_sb = sb("w2_sb", [P, 4, HID2])
        w3_sb = sb("w3_sb", [P, 2])
        b1_sb = sb("b1_sb", [P, 4])
        b2_sb = sb("b2_sb", [P, 2])
        id_sb = sb("id_sb", [P, P])
        pick_sb = sb("pick_sb", [P, 62])
        ids_all = sb("ids_all", [P, TILES, FIELDS], I32)
        ids_now = [sb(f"ids_now{u}", [P, FIELDS], I32) for u in range(2)]

        u_ps = [ctx.enter_context(nc.psum_tensor(f"u_ps{s}", [P, FULL * EMBED], F32)) for s in range(USLOTS)]
        t_ps = ctx.enter_context(nc.psum_tensor("t_ps", [P, 512], F32))[:, 0:GROUP // 2 * P].rearrange(
            "p (m b) -> p m b", b=P)
        mlp_ps = ctx.enter_context(nc.psum_tensor("mlp_ps", [P, 4, P], F32))

        ids_loaded = sem("ids_loaded")
        ids_copied = sem("ids_copied")
        id_loaded = sem("id_loaded")
        weights_loaded = sem("weights_loaded")
        dense_loaded = [sem(f"dense_loaded{u}") for u in range(2)]
        gathered = [[sem(f"gathered{u}_{g}") for g in range(GROUPS)] for u in range(2)]
        k_loaded = [sem(f"k_loaded{s}") for s in range(KSLOTS)]
        k_hi_done = sem("k_hi_done")
        k_lo_done = sem("k_lo_done")
        transposed = sem("transposed")
        hi_done = sem("hi_done")
        lo_done = sem("lo_done")
        doubled = [sem(f"doubled{s}") for s in range(DSLOTS)]
        u_ready = sem("u_ready")
        multiplied = sem("multiplied")
        summed_v = sem("summed_v")
        summed_a = sem("summed_a")
        mlp_mm = sem("mlp_mm")
        mlp_out = sem("mlp_out")
        stored = sem("stored")

        block = ctx.enter_context(nc.Block())

        @block.gpsimd
        def _(pool):
            pool.wait_ge(ids_loaded, 16)

            copies_register = pool.alloc_register("copies")

            def tile(t, u):
                copies = t + 1
                if not isinstance(t, int):
                    pool.reg_mov(copies_register, t + 1)
                    copies = pool.snap(copies_register)
                nc.gpsimd.tensor_copy(ids_now[u][:], ids_all[:, t, :]).then_inc(ids_copied, 1)
                pool.wait_ge(ids_loaded, 16)
                pool.wait_ge(ids_copied, copies)
                for f in range(FIELDS):
                    nc.gpsimd.indirect_dma_start(
                        emb[u][:, f * EMBED:(f + 1) * EMBED], None, tables[f],
                        bass.IndirectOffsetOnAxis(ap=ids_now[u][:, f:f + 1], axis=0),
                    ).then_inc(gathered[u][f // GROUP], 16)

            tile(0, 0)
            tile(1, 1)
            with pool.Fori(1, TILES // 2) as it:
                for u in range(2):
                    t = 2 * it + u
                    pool.wait_ge(multiplied, (t - 1) * NB)
                    tile(t, u)

        @block.sync
        def _(sp):
            sp.dma_start(ids_all[:], ids.rearrange("(t p) f -> p t f", p=P)).then_inc(ids_loaded, 16)
            sp.dma_start(id_sb[:], ident).then_inc(id_loaded, 16)
            sp.dma_start(pick_sb[:], pick).then_inc(id_loaded, 16)

            def double(t, g):
                sp.wait_ge(lo_done, t * GROUPS + g + 1)
                for parity in range(2):
                    for half in range(2):
                        sp.dma_start(
                            twice_t[half * EMBED:(half + 1) * EMBED, g % DSLOTS, :, parity].bitcast(F32),
                            split_t[parity * EMBED:(parity + 1) * EMBED, g % 2].bitcast(F32),
                        ).then_inc(doubled[g % DSLOTS], 16)

            def load_dense(t, u):
                sp.dma_start(h0[u][:, STRAIGHT:], dense[bass.ts(t, P), :]).then_inc(dense_loaded[u], 16)

            def tile(t, u, last=False):
                for g in range(GROUPS):
                    if g + AHEAD < GROUPS:
                        double(t, g + AHEAD)
                    elif not last:
                        double(t + 1, g + AHEAD - GROUPS)
                    if g == 1:
                        load_dense(t, u)

            for c in range(CHUNKS):
                if c >= KSLOTS:
                    sp.wait_ge(k_lo_done, c - KSLOTS + 1)
                sp.dma_start(
                    k_raw[:, c % KSLOTS], k_pairs[:, c * CHUNK * EMBED:(c + 1) * CHUNK * EMBED],
                ).then_inc(k_loaded[c % KSLOTS], 16)
                if c - KSLOTS in EARLY_AT:
                    double(0, EARLY_AT[c - KSLOTS])
            sp.dma_start(w1_sb[:], w1.rearrange("(c p) n -> p c n", p=P)).then_inc(weights_loaded, 16)
            sp.dma_start(w2_sb[:], w2.rearrange("(c p) n -> p c n", p=P)).then_inc(weights_loaded, 16)
            sp.dma_start(w3_sb[:], w3).then_inc(weights_loaded, 16)
            sp.dma_start(b1_sb[:], b1).then_inc(weights_loaded, 16)
            sp.dma_start(b2_sb[:], b2).then_inc(weights_loaded, 16)
            tile(0, 0)
            with sp.Fori(1, TILES - 1, 2) as t1:
                for d in range(2):
                    tile(t1 + d, (1 + d) % 2)
            tile(TILES - 1, (TILES - 1) % 2, last=True)
            sp.wait_ge(stored, 16 * TILES)

        @block.scalar
        def _(act):
            act.sem_inc(mlp_out, 1)

            def round_k(c):
                act.wait_ge(k_loaded[c % KSLOTS], 16 * (c // KSLOTS + 1))
                nc.scalar.activation(
                    k_split[0:EMBED, c * CHUNK * EMBED:(c + 1) * CHUNK * EMBED], k_raw[:, c % KSLOTS], ACT.Copy,
                ).then_inc(k_hi_done, 1)

            def round_group(t, g, u, reused=True):
                act.wait_ge(transposed, t * GROUPS + g + 1)
                if reused:
                    before = g - 2 if g >= 2 else g - 2 + GROUPS
                    turn = (t if g >= 2 else t - 1) * (GROUPS // DSLOTS) + before // DSLOTS
                    act.wait_ge(doubled[before % DSLOTS], 64 * (turn + 1))
                if g < LOW // (GROUP // 2):
                    nc.scalar.activation(low_t[u][:, g * GROUP // 2:(g + 1) * GROUP // 2], t_ps, ACT.Copy)
                nc.scalar.activation(split_t[:, g % 2, :, 0], t_ps, ACT.Copy).then_inc(hi_done, 1)

            def sum_block(t, u, k):
                act.wait_ge(multiplied, t * NB + k + 1)
                for n in range(ON_ACT[k]):
                    product = prod[:, product_slot(u, k), n * EMBED:(n + 1) * EMBED]
                    last = nc.scalar.activation(product, product, ACT.Copy,
                                                accum_out=h0[u][:, COLUMN[k] + n:COLUMN[k] + n + 1])
                last.then_inc(summed_a, 1)

            def mlp_step(t, step):
                act.wait_ge(mlp_mm, STEPS * t + step + 1)
                if step == 0:
                    last = nc.scalar.activation(h0_t[:, 3], mlp_ps[:, 0], ACT.Copy)
                elif step == 1:
                    last = nc.scalar.activation(h0_t[:, 0:3], mlp_ps[:, 0:3], ACT.Copy)
                elif step == 2:
                    for m in range(4):
                        last = nc.scalar.activation(h1_t[:, m], mlp_ps[:, m], ACT.Relu, bias=b1_sb[:, m:m + 1])
                elif step == 3:
                    for m in range(2):
                        last = nc.scalar.activation(h2_t[:, m], mlp_ps[:, m], ACT.Relu, bias=b2_sb[:, m:m + 1])
                else:
                    act.wait_ge(stored, 16 * t)
                    last = nc.scalar.activation(y_row[:], mlp_ps[0:1, 0], ACT.Copy)
                last.then_inc(mlp_out, 1)
                if step == STEPS - 1:
                    act.wait_ge(mlp_out, STEPS * t + STEPS + 1)
                    act.dma_start(out[:, bass.ts(t, P)], y_row[:]).then_inc(stored, 16)

            def tile(t, u, first=False, last=False):
                for g in range(GROUPS):
                    for k in range(FIRST[g], FIRST[g + 1]):
                        if not first and k in MLP_AT:
                            mlp_step(t - 1, MLP_AT[k])
                        if k in ROUND_AT:
                            ahead = ROUND_AT[k] + AHEAD
                            if ahead < GROUPS:
                                round_group(t, ahead, u)
                            elif not last:
                                round_group(t + 1, ahead - GROUPS, 1 - u)
                        if not TURNED[k]:
                            sum_block(t, u, k)

            for c in range(CHUNKS):
                round_k(c)
                if c in EARLY_AT:
                    round_group(0, EARLY_AT[c], 0, reused=EARLY_AT[c] >= 2)
            tile(0, 0, first=True)
            act.wait_ge(weights_loaded, 80)
            with act.Fori(1, TILES - 1, 2) as t1:
                for d in range(2):
                    tile(t1 + d, (1 + d) % 2)
            tile(TILES - 1, (TILES - 1) % 2, last=True)
            for step in range(STEPS):
                mlp_step(TILES - 1, step)

        @block.vector
        def _(dve):
            def split_k(c):
                cols = slice(c * CHUNK * EMBED, (c + 1) * CHUNK * EMBED)
                dve.wait_ge(k_hi_done, c + 1)
                nc.vector.tensor_tensor(k_split[EMBED:P, cols], k_raw[:, c % KSLOTS],
                                        k_split[0:EMBED, cols].bitcast(F32), ALU.subtract).then_inc(k_lo_done, 1)

            def split_group(t, g):
                dve.wait_ge(hi_done, t * GROUPS + g + 1)
                nc.vector.tensor_tensor(split_t[:, g % 2, :, 1], t_ps,
                                        split_t[:, g % 2, :, 0].bitcast(F32), ALU.subtract).then_inc(lo_done, 1)

            def multiply(t, u, k):
                dve.wait_ge(u_ready, t * NB + k + 1)
                before, turn = (k - PSLOTS, t) if k >= PSLOTS else (k - PSLOTS + NB, t - 1)
                if not TURNED[before] and not (k < PSLOTS and isinstance(t, int) and t == 0):
                    dve.wait_ge(summed_a, turn * NS + S_INDEX[before] + 1)
                    dve.wait_ge(summed_v, turn * NS + S_INDEX[before] + 1)
                product = prod[:, product_slot(u, k)]
                if TURNED[k]:
                    last = nc.vector.tensor_tensor(product, u_ps[k % USLOTS][:],
                                                   low_t[u][:].rearrange("p m b -> p (m b)"), ALU.mult)
                at = 0
                for j, i, n in BLOCKS[k] if not TURNED[k] else ():
                    cols = slice(at * EMBED, (at + n) * EMBED)
                    last = nc.vector.tensor_tensor(product[:, cols], u_ps[k % USLOTS][:, cols],
                                                   emb[u][:, i * EMBED:(i + n) * EMBED], ALU.mult)
                    at += n
                last.then_inc(multiplied, 1)

            def sum_block(t, u, k):
                dve.wait_ge(multiplied, t * NB + k + 1)
                product = prod[:, product_slot(u, k), ON_ACT[k] * EMBED:WIDTH[k] * EMBED]
                nc.vector.tensor_reduce(h0[u][:, COLUMN[k] + ON_ACT[k]:COLUMN[k] + WIDTH[k]],
                                        product.rearrange("p (n e) -> p n e", e=EMBED), AX_X, ALU.add,
                                        ).then_inc(summed_v, 1)

            def tile(t, u, last=False):
                for g in range(GROUPS):
                    for k in range(FIRST[g], FIRST[g + 1]):
                        if k in SPLIT_AT:
                            ahead = SPLIT_AT[k] + AHEAD
                            if ahead < GROUPS:
                                split_group(t, ahead)
                            elif not last:
                                split_group(t + 1, ahead - GROUPS)
                        multiply(t, u, k)
                        if k > 0 and not TURNED[k - 1]:
                            sum_block(t, u, k - 1)
                if not TURNED[NB - 1]:
                    sum_block(t, u, NB - 1)

            for c in range(CHUNKS):
                split_k(c)
                if c in EARLY_AT:
                    split_group(0, EARLY_AT[c])
            dve.wait_ge(k_lo_done, CHUNKS)
            tile(0, 0)
            with dve.Fori(1, TILES - 1, 2) as t1:
                for d in range(2):
                    tile(t1 + d, (1 + d) % 2)
            tile(TILES - 1, (TILES - 1) % 2, last=True)

        @block.tensor
        def _(pe):
            def transpose_group(t, g, u):
                turn = (t // 2 if isinstance(t, int) else (t - u) // 2) + 1
                pe.wait_ge(gathered[u][g], 16 * GROUP * turn)
                if g > 0 or not isinstance(t, int) or t > 0:
                    pe.wait_ge(lo_done, t * GROUPS + g)
                for m in range(GROUP // 2):
                    f = GROUP * g + 2 * m
                    last = nc.tensor.transpose(t_ps[:, m], emb[u][:, f * EMBED:(f + 2) * EMBED], id_sb[:])
                last.then_inc(transposed, 1)

            def block_u(t, k):
                if k >= USLOTS or not isinstance(t, int) or t > 0:
                    pe.wait_ge(multiplied, t * NB + k + 1 - USLOTS)
                at = 0
                for j, i, n in BLOCKS[k]:
                    slot = j // GROUP % DSLOTS
                    if TURNED[k]:
                        for m in range(LOW):
                            for part in range(2):
                                last = nc.tensor.matmul(
                                    u_ps[k % USLOTS][:, m * P:(m + 1) * P],
                                    k_split[:, pair(j, 2 * m) * EMBED:pair(j, 2 * m + 2) * EMBED],
                                    twice_t[:, slot, j % GROUP // 2, j % 2, part],
                                    start=(part == 0), stop=(part == 1))
                        continue
                    done = 0
                    while done < n:
                        m = min(n - done, BANK - (at + done) % BANK)
                        dst = u_ps[k % USLOTS][:, (at + done) * EMBED:(at + done + m) * EMBED]
                        src = k_split[:, (pair(j, i) + done) * EMBED:(pair(j, i) + done + m) * EMBED]
                        for part in range(2):
                            last = nc.tensor.matmul(dst, twice_t[:, slot, j % GROUP // 2, j % 2, part], src,
                                                    start=(part == 0), stop=(part == 1))
                        done += m
                    at += n
                last.then_inc(u_ready, 1)

            def sum_turned(t, u, k):
                if T_INDEX[k] == 0:
                    pe.wait_ge(mlp_out, STEPS * t + 1)
                pe.wait_ge(multiplied, t * NB + k + 1)
                for m in range(LOW):
                    g = T_INDEX[k] * LOW + m
                    quad, s = g % QUADS, g // QUADS
                    last = nc.tensor.matmul(mlp_ps[32 * quad:32 * quad + 32, 0], pick_sb[:, 30 - 2 * s:62 - 2 * s],
                                            prod[:, product_slot(u, k), m * P:(m + 1) * P],
                                            start=(s == 0), stop=(s == 15))
                if T_INDEX[k] == NT - 1:
                    last.then_inc(mlp_mm, 1)

            def mlp_step(t, u, step):
                pe.wait_ge(mlp_out, STEPS * t + step + 1)
                if step == 1:
                    pe.wait_ge(summed_v, (t + 1) * NS)
                    pe.wait_ge(summed_a, (t + 1) * NS)
                    turn = (t // 2 if isinstance(t, int) else (t - u) // 2) + 1
                    pe.wait_ge(dense_loaded[u], 16 * turn)
                    for c in range(3):
                        last = nc.tensor.transpose(mlp_ps[:, c], h0[u][:, c * P:(c + 1) * P], id_sb[:])
                elif step == 2:
                    for m in range(4):
                        for c in range(4):
                            last = nc.tensor.matmul(mlp_ps[:, m], w1_sb[:, c, m * P:(m + 1) * P], h0_t[:, c],
                                                    start=(c == 0), stop=(c == 3))
                elif step == 3:
                    for m in range(2):
                        for c in range(4):
                            last = nc.tensor.matmul(mlp_ps[:, m], w2_sb[:, c, m * P:(m + 1) * P], h1_t[:, c],
                                                    start=(c == 0), stop=(c == 3))
                else:
                    for c in range(2):
                        last = nc.tensor.matmul(mlp_ps[0:1, 0], w3_sb[:, c:c + 1], h2_t[:, c],
                                                start=(c == 0), stop=(c == 1))
                last.then_inc(mlp_mm, 1)

            def tile(t, u, first=False, last=False):
                for g in range(GROUPS):
                    for k in range(FIRST[g], FIRST[g + 1]):
                        if not first and MLP_AT.get(k, 0) > 0:
                            mlp_step(t - 1, 1 - u, MLP_AT[k])
                        if k == FIRST[g]:
                            pe.wait_ge(doubled[g % DSLOTS], 64 * (t * (GROUPS // DSLOTS) + g // DSLOTS + 1))
                        block_u(t, k)
                        if k >= USLOTS and TURNED[k - USLOTS]:
                            sum_turned(t, u, k - USLOTS)
                        elif k < USLOTS and not first and TURNED[k - USLOTS + NB]:
                            sum_turned(t - 1, 1 - u, k - USLOTS + NB)
                        if k in TURN_AT:
                            ahead = TURN_AT.index(k) + AHEAD
                            if ahead < GROUPS:
                                transpose_group(t, ahead, u)
                            elif not last:
                                transpose_group(t + 1, ahead - GROUPS, 1 - u)

            pe.wait_ge(id_loaded, 32)
            for g in range(AHEAD):
                transpose_group(0, g, 0)
            pe.wait_ge(k_lo_done, CHUNKS)
            tile(0, 0, first=True)
            pe.wait_ge(weights_loaded, 80)
            with pe.Fori(1, TILES - 1, 2) as t1:
                for d in range(2):
                    tile(t1 + d, (1 + d) % 2)
            tile(TILES - 1, (TILES - 1) % 2, last=True)
            for k in range(NB - USLOTS, NB):
                if TURNED[k]:
                    sum_turned(TILES - 1, (TILES - 1) % 2, k)
            for step in range(1, STEPS):
                mlp_step(TILES - 1, (TILES - 1) % 2, step)


def by_partition(v):
    return np.ascontiguousarray(np.asarray(v).reshape(-1, P).T)


def kernel(**inputs):
    import concourse.bacc as bacc
    from concourse.bass_utils import run_bass_kernel_spmd

    order = [i * (2 * FIELDS - i - 1) // 2 + j - i - 1 for j in range(FIELDS) for i in range(j)]
    w1 = np.asarray(inputs["W_top1"])
    k = np.asarray(inputs["L0_rec_kernel"])
    pick = np.zeros((P, 62), np.float32)
    pick[:EMBED, 30] = 1
    pick[EMBED:, 31] = 1
    arrays = {
        "ids": np.asarray(inputs["ids"]),
        "k_pairs": np.ascontiguousarray(k[:, order, :]).reshape(EMBED, PAIRS * EMBED),
        "dense": np.asarray(inputs["dense_ctx"]),
        "w1": w1[w1_rows()],
        "b1": by_partition(inputs["b_top1"]),
        "w2": np.asarray(inputs["W_top2"]),
        "b2": by_partition(inputs["b_top2"]),
        "w3": by_partition(inputs["W_top3"]),
        "ident": np.eye(P, dtype=np.float32),
        "pick": pick,
    }
    for f in range(FIELDS):
        arrays[f"tbl_{f}"] = np.asarray(inputs[f"tbl_{f}"])
    nc = bacc.Bacc("TRN2", target_bir_lowering=False, num_devices=1)
    ap = {n: nc.dram_tensor(n, a.shape, mybir.dt.from_np(a.dtype), kind="ExternalInput").ap()
          for n, a in arrays.items()}
    out = nc.dram_tensor("out", (1, BATCH), F32, kind="ExternalOutput").ap()
    build(nc, ap["ids"], [ap[f"tbl_{f}"] for f in range(FIELDS)], ap["k_pairs"], ap["dense"],
          ap["w1"], ap["b1"], ap["w2"], ap["b2"], ap["w3"], ap["ident"], ap["pick"], out)
    r = run_bass_kernel_spmd(nc, [arrays], core_ids=[0])
    return r.results[0]["out"].reshape(BATCH, 1)
```
